# Optimizing a Trainium2 kernel written in Bass

```python
import numpy as np
import jax
import jax.numpy as jnp

def _softmax(x, axis=-1):
    return jax.nn.softmax(x, axis=axis)

def _gelu(x):
    return jax.nn.gelu(x, approximate=True)

def _silu(x):
    return jax.nn.silu(x)

def _sigmoid(x):
    return jax.nn.sigmoid(x)

def _layernorm(x, axis=-1, eps=1e-05):
    m = jnp.mean(x, axis=axis, keepdims=True)
    v = jnp.var(x, axis=axis, keepdims=True)
    return (x - m) / jnp.sqrt(v + eps)

def _scatter_add(tgt, idx, src, axis=0):
    return tgt.at[idx].add(src)

def _segment_sum(src, seg, n):
    return jax.ops.segment_sum(src, seg, n)
kernel_name = 'mk_adj_resnorm_d2_adj_r2_e9d578'

def setup_inputs(seed: int=0):
    np.random.seed(seed)
    _w = jnp.asarray

    def _rec_inputs():
        import jax
        import jax.numpy as jnp
        _gk = jax.random.key(seed)
        x = -0.0005207 + 1.001 * jax.random.normal(jax.random.fold_in(_gk, 1), (8192, 128), jnp.float32)
        _a = jax.random.bernoulli(jax.random.fold_in(_gk, 2), 0.000244141, (8192, 8192))
        _a = jnp.logical_or(_a, jnp.eye(8192, dtype=bool))
        _af = _a.astype(jnp.float32)
        _af = _af * jax.random.uniform(jax.random.fold_in(_gk, 3), (8192, 8192), jnp.float32, 0.05, 1)
        adj = _af
        return (x, adj)
    x, adj = _rec_inputs()

    def _L0_gnn_setup():
        import jax, jax.numpy as jnp
        import numpy as np
        ALPHA = 0.1
        N, F = (8192, 128)
        key = jax.random.key(seed)
        k1, k2, k3 = jax.random.split(key, 3)
        x = jax.random.normal(k1, (N, F), dtype=jnp.float32)
        adj = jax.random.uniform(k2, (N, N), dtype=jnp.float32)
        h = jax.random.normal(k3, (N, F), dtype=jnp.float32)
        return {'x': x, 'adj': adj, 'h': h}
    _L0_gnn_all = _L0_gnn_setup()
    _L0_gnn_in = {k: v for k, v in _L0_gnn_all.items() if k in ('h',)}
    del _L0_gnn_all

    def _L1_gnn_setup():
        import jax, jax.numpy as jnp
        import numpy as np
        N = 4096
        IN_F = 128
        OUT_F = 128
        key = jax.random.key(seed)
        k1, k2, k3, k4 = jax.random.split(key, 4)
        x = jax.random.normal(k1, (N, IN_F), dtype=jnp.float32)
        adj = jax.random.uniform(k2, (N, N), dtype=jnp.float32)
        lim = 1.0 / np.sqrt(IN_F)
        W = jax.random.uniform(k3, (OUT_F, IN_F), dtype=jnp.float32, minval=-lim, maxval=lim)
        b = jax.random.uniform(k4, (OUT_F,), dtype=jnp.float32, minval=-lim, maxval=lim)
        return {'x': x, 'adj': adj, 'W': W, 'b': b}
    _L1_gnn_all = _L1_gnn_setup()
    _L1_gnn_in = {k: v for k, v in _L1_gnn_all.items() if k in ('W', 'b')}
    del _L1_gnn_all
    return {'x': x, 'adj': adj, 'L0_gnn_h': _L0_gnn_in['h'], 'L1_gnn_W': _L1_gnn_in['W'], 'L1_gnn_b': _L1_gnn_in['b']}

def reference(x, adj, L0_gnn_h, L1_gnn_W, L1_gnn_b):
    import jax
    import jax.numpy as jnp

    def _L0_gnn_ref(x, adj, h):
        import jax, jax.numpy as jnp
        import numpy as np
        ALPHA = 0.1
        N, F = (8192, 128)
        return (1.0 - ALPHA) * (adj @ x) + ALPHA * h

    def _L1_gnn_ref(x, adj, W, b):
        import jax, jax.numpy as jnp
        import numpy as np
        N = 4096
        IN_F = 128
        OUT_F = 128
        h = x @ W.T + b
        a = adj + jnp.eye(adj.shape[0], dtype=adj.dtype)
        rowsum = a.sum(axis=1)
        r_inv_sqrt = jnp.where(rowsum > 0, rowsum ** (-0.5), 0.0)
        a_norm = a * r_inv_sqrt[:, None] * r_inv_sqrt[None, :]
        return a_norm @ h
    x = _layernorm(x + _L0_gnn_ref(x, adj, L0_gnn_h), axis=-1)
    x = _layernorm(x + _L1_gnn_ref(x, adj, L1_gnn_W, L1_gnn_b), axis=-1)
    return x

_drawn_inputs = setup_inputs


def setup_inputs(seed=0):
    import zlib

    import numpy as np

    out = dict(_drawn_inputs(seed))
    spreads = {}
    factors = {}
    for name, (base, spread) in spreads.items():
        noise = np.random.default_rng([zlib.crc32(name.encode()), seed]).standard_normal(out[name].shape)
        drawn = base * np.exp(spread * noise) if base else spread * noise
        out[name] = jnp.asarray(drawn.astype(out[name].dtype))
    for name, factor in factors.items():
        out[name] = (out[name] * factor).astype(out[name].dtype)
    return out
```

```python
import concourse.bass as bass
from concourse import mybir
from contextlib import ExitStack

P = 128
GROUP = 1024
CHUNKS = GROUP // P
UNITS = 4
PER_UNIT = CHUNKS // UNITS
BANK = 512
HALVES = GROUP // BANK
EPS = 1e-5
TINY = 1.17549435e-38


def graph_kernel(nc, adj_blocks, x, h, w_t, bias, out, res):
    fp32, fp32r = mybir.dt.float32, mybir.dt.float32r
    ALU = mybir.AluOpType
    ACT = mybir.ActivationFunctionType
    NG = x.shape[1] // CHUNKS
    assert NG % 2 == 0 and UNITS * PER_UNIT == CHUNKS

    def block_a(I, p):
        return I * NG + p

    class BlockCount:

        def __init__(self, eng, first):
            self.eng, self.reg = eng, eng.alloc_register("blocks_done")
            eng.reg_mov(self.reg, first)

        def now(self):
            return self.eng.snap(self.reg, min_val=NG * NG, max_val=BLOCKS)

        def step(self):
            self.eng.reg_add(self.reg, self.reg, 1)

    def fused(I, p):
        if isinstance(p, int):
            return isinstance(I, int) and I + p >= NG
        if isinstance(I, int) and I in (0, NG - 1):
            return I > 0
        return I + p >= NG

    BLOCKS = NG * NG + NG * (NG + 1) // 2

    with ExitStack() as ctx:
        def sb(name, shape, dt=fp32):
            return ctx.enter_context(nc.sbuf_tensor(name, shape, dt))

        def ps(name, shape):
            return ctx.enter_context(nc.psum_tensor(name, shape, fp32))

        def sem(name):
            return ctx.enter_context(nc.semaphore(name))

        xs = sb("xs", [P, NG * CHUNKS, P])
        g = sb("g", [P, NG * CHUNKS, P])
        raw = sb("raw", [P, UNITS, PER_UNIT, GROUP])
        adj_hi = sb("adj_hi", [P, UNITS, PER_UNIT, GROUP], fp32r)
        adj_lo = sb("adj_lo", [P, UNITS, PER_UNIT, GROUP], fp32r)
        x_hi = sb("x_hi", [P, UNITS, PER_UNIT, P], fp32r)
        x_lo = sb("x_lo", [P, UNITS, PER_UNIT, P], fp32r)
        g_hi = sb("g_hi", [P, UNITS, PER_UNIT, P], fp32r)
        g_lo = sb("g_lo", [P, UNITS, PER_UNIT, P], fp32r)
        addend = sb("addend", [P, CHUNKS, P])
        v = sb("v", [P, CHUNKS, P])
        x1 = sb("x1", [P, CHUNKS, P])
        sum1_t = sb("sum1_t", [P, GROUP])
        sum2_t = sb("sum2_t", [P, GROUP])
        stats = sb("stats", [P, CHUNKS, 6])
        mean_var = sb("mean_var", [P, CHUNKS, 2])
        roots = sb("roots", [P, 2, CHUNKS])
        positive = sb("positive", [P, CHUNKS])
        r = sb("r", [P, NG * CHUNKS])
        ident = sb("ident", [P, P])
        weights = sb("weights", [P, P])
        bias_row = sb("bias_row", [P, P])
        zeros = sb("zeros", [P, BANK], mybir.dt.bfloat16)

        acc = [ps(f"acc{q}", [P, GROUP]) for q in range(2)]
        acc2 = ps("acc2", [P, GROUP])
        sum2 = ps("sum2", [P, CHUNKS, P])

        def scratch(q):
            return acc[q][:, :].rearrange("p (c f) -> p c f", f=P)

        x_loaded = [sem(f"x_loaded{c}") for c in range(NG)]
        consts_loaded = sem("consts_loaded")
        consts_built = sem("consts_built")
        x_shifted = sem("x_shifted")
        adj_loaded = [sem(f"adj_loaded{k}") for k in range(UNITS)]
        hi_ready = sem("hi_ready")
        lo_ready = sem("lo_ready")
        unit_done = sem("unit_done")
        addend_loaded = sem("addend_loaded")
        sums_copied = sem("sums_copied")
        sums_transposed = sem("sums_transposed")
        squares_ready = sem("squares_ready")
        roots_ready = sem("roots_ready")
        x1_ready = sem("x1_ready")
        x1_transposed = sem("x1_transposed")
        x1_t_copied = sem("x1_t_copied")
        h_ready = sem("h_ready")
        g_ready = sem("g_ready")
        result_ready = sem("result_ready")
        result_stored = sem("result_stored")
        dve_step = sem("dve_step")

        block = ctx.enter_context(nc.Block())

        @block.sync
        def _(sp):
            def load_block(I, p, b):
                for k in range(UNITS):
                    sp.wait_ge(lo_ready, b * UNITS + k + 1)
                    src = adj_blocks[bass.ds((I * NG + p) * UNITS + k, 1), :, :].rearrange("o p n -> (o p) n")
                    sp.dma_start(raw[:, k, :, :].rearrange("p j i -> p (j i)"), src).then_inc(adj_loaded[k], 16)

            with sp.Fori(0, NG) as I:
                with sp.Fori(0, NG) as p:
                    load_block(I, p, block_a(I, p))
            count = BlockCount(sp, block_a(NG, 0))
            with sp.Fori(0, NG) as I:
                with sp.Fori(0, NG - I) as p:
                    load_block(I, p, count.now())
                    count.step()

        @block.gpsimd
        def _(pool):
            pool.memset(ident[:, :], 0.0).then_inc(consts_built, 1)
            pool.memset(zeros[:, :], 0.0).then_inc(consts_built, 1)
            pool.wait_ge(consts_built, 2)
            pool.affine_select(out=ident[:, :], in_=ident[:, :], compare_op=ALU.not_equal, fill=1.0, base=0,
                               pattern=[[-1, P]], channel_multiplier=1).then_inc(consts_built, 1)
            for c in range(NG):
                part = xs[:, c * CHUNKS:(c + 1) * CHUNKS, :]
                pool.wait_ge(x_loaded[c], 16)
                pool.tensor_tensor(part[:, :, 1:P], part[:, :, 1:P],
                                   part[:, :, 0:1].to_broadcast([P, CHUNKS, P - 1]),
                                   ALU.subtract).then_inc(x_shifted, 1)
                pool.wait_ge(x_shifted, 2 * c + 1)
                pool.memset(part[:, :, 0:1], 1.0).then_inc(x_shifted, 1)

            def rows(tensor, I):
                return tensor[:, bass.ds(I * CHUNKS, CHUNKS), :]

            def load_addend(tensor, I):
                pool.dma_start(addend[:, :, :], rows(tensor, I)).then_inc(addend_loaded, 16)

            def store(tensor, I, tile, s):
                pool.wait_ge(result_ready, s + 2)
                pool.dma_start(rows(tensor, I), tile[:, :, :]).then_inc(result_stored, 16)
                pool.wait_ge(result_stored, s * 16 + 16)

            load_addend(h, 0)
            with pool.Fori(0, NG - 1) as I:
                store(res, I, v, I)
                load_addend(h, I + 1)
            store(res, NG - 1, v, NG - 1)
            load_addend(res, 0)
            with pool.Fori(0, NG - 1) as I:
                store(out, I, x1, I + NG)
                load_addend(res, I + 1)
            store(out, NG - 1, x1, 2 * NG - 1)

        @block.scalar
        def _(act):
            for c in range(NG):
                part = slice(c * CHUNKS, (c + 1) * CHUNKS)
                act.dma_start(xs[:, part, :], x[:, part, :]).then_inc(x_loaded[c], 16)
            act.dma_start(weights[:, :], w_t).then_inc(consts_loaded, 16)
            act.dma_start(bias_row[:, :], bias.to_broadcast([P, P])).then_inc(consts_loaded, 16)

            def hi_parts(b, k, K, with_x, fused):
                act.wait_ge(unit_done, b * UNITS + k + 1)
                act.wait_ge(adj_loaded[k], b * 16 + 16)
                last = act.activation(adj_hi[:, k, :, :], raw[:, k, :, :], ACT.Copy)
                chunks = bass.ds(K * CHUNKS + k * PER_UNIT, PER_UNIT)
                if fused is True:
                    act.wait_ge(g_ready, K + 1)
                    last = act.activation(g_hi[:, k, :, :], g[:, chunks, :], ACT.Copy)
                elif fused is not False:
                    with act.If(fused):
                        act.wait_ge(g_ready, K + 1)
                        act.activation(g_hi[:, k, :, :], g[:, chunks, :], ACT.Copy)
                if with_x:
                    last = act.activation(x_hi[:, k, :, :], xs[:, chunks, :], ACT.Copy)
                last.then_inc(hi_ready, 1)

            def copy_sums(q, s, b_end, phase_a):
                act.wait_ge(unit_done, b_end * UNITS + UNITS)
                last = act.activation(sum1_t[:, :], acc[q][:, :], ACT.Copy)
                if phase_a:
                    last = act.activation(sum2_t[:, :], acc2[:, :], ACT.Copy)
                last.then_inc(sums_copied, 1)

            def take_roots(s):
                act.wait_ge(squares_ready, s + 1)
                act.activation(roots[:, :, :], roots[:, :, :], ACT.Sqrt).then_inc(roots_ready, 1)

            def copy_x1_t(q, s):
                act.wait_ge(x1_transposed, s + 1)
                act.activation(sum1_t[:, :], acc[q][:, :], ACT.Copy).then_inc(x1_t_copied, 1)

            def group_a(I, q, hosts):
                for p in range(2):
                    b, K = block_a(I, p), (I + p) % NG
                    for k in range(UNITS):
                        if not hosts:
                            act.wait_ge(x_shifted, 2 * p + 2)
                        hi_parts(b, k, K, True, fused(I, p))
                        if p == 1 and k == 0 and hosts:
                            take_roots(I - 1)
                        if p == 1 and k == 1 and hosts:
                            copy_x1_t(1 - q, I - 1)
                    if p == 0 and hosts:
                        copy_sums(1 - q, I - 1, I * NG, True)
                with act.Fori(2, NG) as p:
                    for k in range(UNITS):
                        if not hosts:
                            act.wait_ge(x_shifted, p * 2 + 2)
                        hi_parts(block_a(I, p), k, (I + p) % NG, True, fused(I, p))

            def group_b(I, q, more):
                b = count.now()
                for k in range(UNITS):
                    hi_parts(b, k, I, False, True)
                copy_sums(1 - q, I + (NG - 1), b, False)
                take_roots(I + (NG - 1))
                count.step()
                if more:
                    with act.Fori(1, NG - I) as p:
                        b = count.now()
                        for k in range(UNITS):
                            hi_parts(b, k, (I + p) % NG, False, True)
                        count.step()

            group_a(0, 0, False)
            with act.Fori(0, NG // 2 - 1) as pair:
                group_a(pair * 2 + 1, 1, True)
                group_a(pair * 2 + 2, 0, True)
            group_a(NG - 1, 1, True)
            for p in range(2):
                for k in range(UNITS):
                    hi_parts(block_a(NG, p), k, p, False, True)
                    if p == 1 and k == 0:
                        take_roots(NG - 1)
                    if p == 1 and k == 1:
                        copy_x1_t(1, NG - 1)
                if p == 0:
                    copy_sums(1, NG - 1, NG * NG, True)
            with act.Fori(2, NG) as p:
                for k in range(UNITS):
                    hi_parts(block_a(NG, p), k, p, False, True)
            count = BlockCount(act, block_a(NG + 1, 0))
            with act.Fori(0, NG // 2 - 1) as pair:
                group_b(pair * 2 + 1, 1, True)
                group_b(pair * 2 + 2, 0, True)
            group_b(NG - 1, 1, False)
            copy_sums(1, 2 * NG - 1, BLOCKS, False)
            take_roots(2 * NG - 1)

        @block.vector
        def _(dve):
            STEPS_A, STEPS_B = 7, 4

            def lo_parts(b, k, K, with_x, fused):
                chunks = bass.ds(K * CHUNKS + k * PER_UNIT, PER_UNIT)
                dve.wait_ge(hi_ready, b * UNITS + k + 1)

                last = dve.tensor_tensor(adj_lo[:, k, :, :], raw[:, k, :, :], adj_hi[:, k, :, :].bitcast(fp32),
                                         ALU.subtract)

                def g_part():
                    return dve.tensor_tensor(g_lo[:, k, :, :], g[:, chunks, :], g_hi[:, k, :, :].bitcast(fp32),
                                             ALU.subtract)

                if fused is True:
                    last = g_part()
                elif fused is not False:
                    with dve.If(fused):
                        g_part()
                if with_x:
                    last = dve.tensor_tensor(x_lo[:, k, :, :], xs[:, chunks, :], x_hi[:, k, :, :].bitcast(fp32),
                                             ALU.subtract)
                last.then_inc(lo_ready, 1)

            def step(instruction, count):
                instruction.then_inc(dve_step, 1)
                dve.wait_ge(dve_step, count)

            def norm(s, done, row_sums):
                for c in range(CHUNKS):
                    last = dve.bn_stats(stats[:, c, :], v[:, c, :])
                step(last, done + 1)
                row_sums()
                for c in range(CHUNKS):
                    last = dve.bn_aggr(mean_var[:, c, :], stats[:, c, :])
                step(last, done + 2)
                dve.tensor_scalar(roots[:, 1, :], mean_var[:, :, 1], EPS, None, ALU.add).then_inc(squares_ready, 1)
                dve.wait_ge(roots_ready, s + 1)
                step(dve.reciprocal(roots[:, :, :], roots[:, :, :]), done + 3)
                for c in range(CHUNKS):
                    last = dve.tensor_scalar(x1[:, c, :], v[:, c, :], mean_var[:, c, 0:1], roots[:, 1, c:c + 1],
                                             ALU.subtract, ALU.mult)
                return last

            def first_norm(q, s):
                y = scratch(q)
                own = bass.ds(s * CHUNKS, CHUNKS)
                dve.wait_ge(addend_loaded, s * 16 + 16)
                step(dve.scalar_tensor_tensor(v[:, :, :], addend[:, :, :], 0.1, xs[:, own, :],
                                              ALU.mult, ALU.add), s * STEPS_A + 1)
                dve.wait_ge(sums_transposed, s + 1)
                dve.scalar_tensor_tensor(v[:, :, 1:P], y[:, :, 1:P], 0.9, v[:, :, 1:P], ALU.mult, ALU.add)
                dve.tensor_scalar(positive[:, :], y[:, :, 0], 1.0, 0.0, ALU.add, ALU.is_gt)
                step(dve.tensor_scalar(v[:, :, 0], addend[:, :, 0], 0.1, None, ALU.mult), s * STEPS_A + 2)
                norm(s, s * STEPS_A + 2,
                     lambda: dve.tensor_scalar(roots[:, 0, :], y[:, :, 0], 1.0, TINY, ALU.add, ALU.max)
                     ).then_inc(x1_ready, 1)
                dve.tensor_tensor(r[:, own], roots[:, 0, :], positive[:, :], ALU.mult)

            def features_2(q, s):
                own = bass.ds(s * CHUNKS, CHUNKS)
                dve.wait_ge(h_ready, s + 1)
                step(dve.tensor_tensor(v[:, :, :], scratch(q),
                                       bias_row[:, :].unsqueeze(1).to_broadcast([P, CHUNKS, P]), ALU.add), s * STEPS_A + 6)
                dve.tensor_tensor(g[:, own, :], v[:, :, :],
                                  r[:, own].unsqueeze(2).to_broadcast([P, CHUNKS, P]),
                                  ALU.mult).then_inc(g_ready, 1)

            def start_layer_2(s):
                dve.wait_ge(g_ready, s + 1)
                for c in range(CHUNKS):
                    mine = s * CHUNKS + c
                    last = dve.scalar_tensor_tensor(v[:, c, :], g[:, bass.ds(mine, 1), :].rearrange("p o f -> p (o f)"),
                                                    r[:, bass.ds(mine, 1)], x1[:, c, :], ALU.mult, ALU.add)
                step(last, s * STEPS_A + 7)
                for c in range(CHUNKS):
                    last = dve.scalar_tensor_tensor(v[:, c, :], sum2[:, c, :], r[:, bass.ds(s * CHUNKS + c, 1)],
                                                    v[:, c, :], ALU.mult, ALU.add)
                last.then_inc(result_ready, 1)

            def second_norm(q, I):
                s = I + NG
                dve.wait_ge(addend_loaded, s * 16 + 16)
                dve.wait_ge(sums_transposed, s + 1)
                y = scratch(q)
                for c in range(CHUNKS):
                    last = dve.scalar_tensor_tensor(v[:, c, :], y[:, c, :], r[:, bass.ds(I * CHUNKS + c, 1)],
                                                    addend[:, c, :], ALU.mult, ALU.add)
                step(last, I * STEPS_B + (NG * STEPS_A + 1))
                norm(s, I * STEPS_B + (NG * STEPS_A + 1), lambda: dve.memset(roots[:, 0, :], 1.0)).then_inc(result_ready, 1)

            def group_a(I, q, hosts):
                for p in range(2):
                    for k in range(UNITS):
                        lo_parts(block_a(I, p), k, (I + p) % NG, True, fused(I, p))
                        if p == 1 and hosts:
                            if k == 1:
                                features_2(1 - q, I - 1)
                            if k == 2:
                                start_layer_2(I - 1)
                    if p == 0 and hosts:
                        first_norm(1 - q, I - 1)
                with dve.Fori(2, NG) as p:
                    for k in range(UNITS):
                        lo_parts(block_a(I, p), k, (I + p) % NG, True, fused(I, p))

            def group_b(I, q, more):
                b = count.now()
                for k in range(UNITS):
                    lo_parts(b, k, I, False, True)
                second_norm(1 - q, I - 1)
                count.step()
                if more:
                    with dve.Fori(1, NG - I) as p:
                        b = count.now()
                        for k in range(UNITS):
                            lo_parts(b, k, (I + p) % NG, False, True)
                        count.step()

            dve.sem_inc(lo_ready, UNITS)
            dve.sem_inc(result_ready, 1)
            dve.wait_ge(consts_loaded, 32)
            group_a(0, 0, False)
            with dve.Fori(0, NG // 2 - 1) as pair:
                group_a(pair * 2 + 1, 1, True)
                group_a(pair * 2 + 2, 0, True)
            group_a(NG - 1, 1, True)
            for p in range(2):
                for k in range(UNITS):
                    lo_parts(block_a(NG, p), k, p, False, True)
                    if p == 1 and k == 1:
                        features_2(1, NG - 1)
                    if p == 1 and k == 2:
                        start_layer_2(NG - 1)
                if p == 0:
                    first_norm(1, NG - 1)
            with dve.Fori(2, NG) as p:
                for k in range(UNITS):
                    lo_parts(block_a(NG, p), k, p, False, True)
            count = BlockCount(dve, block_a(NG + 1, 0))
            with dve.Fori(0, NG // 2 - 1) as pair:
                group_b(pair * 2 + 1, 1, True)
                group_b(pair * 2 + 2, 0, True)
            group_b(NG - 1, 1, False)
            second_norm(1, NG - 1)

        @block.tensor
        def _(pe):
            def products(to, hi, lo, k, start):
                for half in range(HALVES):
                    cols = slice(half * BANK, (half + 1) * BANK)
                    for j in range(PER_UNIT):
                        fresh = start and k == 0 and j == 0
                        pe.matmul(to[:, cols], lo[:, k, j, :], adj_hi[:, k, j, cols], start=fresh, stop=False,
                                  skip_group_check=True)
                        pe.matmul(to[:, cols], hi[:, k, j, :], adj_hi[:, k, j, cols], start=False, stop=False,
                                  skip_group_check=True)
                        last = pe.matmul(to[:, cols], hi[:, k, j, :], adj_lo[:, k, j, cols], start=False, stop=True,
                                         skip_group_check=True)
                return last

            def unit_a(b, k, q, start, fused):
                pe.wait_ge(lo_ready, b * UNITS + (k + 1 + UNITS))
                if fused is not False:
                    with pe.If(fused):
                        products(acc2, g_hi, g_lo, k, False)
                products(acc[q], x_hi, x_lo, k, start).then_inc(unit_done, 1)

            def unit_b(b, k, q, start):
                pe.wait_ge(lo_ready, b * UNITS + (k + 1 + UNITS))
                products(acc[q], g_hi, g_lo, k, start).then_inc(unit_done, 1)

            def transpose(to, source):
                for c in range(CHUNKS):
                    last = pe.transpose(to[:, c, :], source(c), ident[:, :])
                return last

            def transpose_sums(q, s, phase_a):
                pe.wait_ge(sums_copied, s + 1)
                if phase_a:
                    transpose(sum2, lambda c: sum2_t[:, c * P:(c + 1) * P])
                transpose(scratch(q), lambda c: sum1_t[:, c * P:(c + 1) * P]).then_inc(sums_transposed, 1)

            def transpose_x1(q, s):
                pe.wait_ge(x1_ready, s + 1)
                transpose(scratch(q), lambda c: x1[:, c, :]).then_inc(x1_transposed, 1)

            def features_2(q, s):
                pe.wait_ge(x1_t_copied, s + 1)
                for c in range(CHUNKS):
                    last = pe.matmul(scratch(q)[:, c, :], sum1_t[:, c * P:(c + 1) * P], weights[:, :],
                                     start=True, stop=True)
                last.then_inc(h_ready, 1)

            def clear_acc2():
                for half in range(HALVES):
                    pe.matmul(acc2[:, half * BANK:(half + 1) * BANK], zeros[:, 0:P], zeros[:, :],
                              start=True, stop=False, skip_group_check=True)

            def group_a(I, q, hosts):
                if not hosts:
                    clear_acc2()
                else:
                    pe.wait_ge(result_ready, I)
                for p in range(2):
                    for k in range(UNITS):
                        unit_a(block_a(I, p), k, q, p == 0, fused(I, p))
                        if p == 0 and hosts:
                            if k == 0:
                                transpose_sums(1 - q, I - 1, True)
                                clear_acc2()
                            if k == 2:
                                transpose_x1(1 - q, I - 1)
                            if k == 3:
                                features_2(1 - q, I - 1)
                with pe.Fori(2, NG) as p:
                    for k in range(UNITS):
                        unit_a(block_a(I, p), k, q, False, fused(I, p))

            def group_b(I, q, more):
                pe.wait_ge(result_ready, I + NG)
                b = count.now()
                for k in range(UNITS):
                    unit_b(b, k, q, True)
                    if k == 0:
                        transpose_sums(1 - q, I + (NG - 1), False)
                count.step()
                if more:
                    with pe.Fori(1, NG - I) as p:
                        b = count.now()
                        for k in range(UNITS):
                            unit_b(b, k, q, False)
                        count.step()

            pe.sem_inc(unit_done, UNITS)
            pe.wait_ge(consts_built, 3)
            pe.wait_ge(consts_loaded, 32)
            group_a(0, 0, False)
            with pe.Fori(0, NG // 2 - 1) as pair:
                group_a(pair * 2 + 1, 1, True)
                group_a(pair * 2 + 2, 0, True)
            group_a(NG - 1, 1, True)
            pe.wait_ge(result_ready, NG)
            for p in range(2):
                for k in range(UNITS):
                    unit_b(block_a(NG, p), k, 0, p == 0)
                    if p == 0 and k == 0:
                        transpose_sums(1, NG - 1, True)
                    if p == 0 and k == 2:
                        transpose_x1(1, NG - 1)
                    if p == 0 and k == 3:
                        features_2(1, NG - 1)
            with pe.Fori(2, NG) as p:
                for k in range(UNITS):
                    unit_b(block_a(NG, p), k, 0, False)
            count = BlockCount(pe, block_a(NG + 1, 0))
            with pe.Fori(0, NG // 2 - 1) as pair:
                group_b(pair * 2 + 1, 1, True)
                group_b(pair * 2 + 2, 0, True)
            group_b(NG - 1, 1, False)
            transpose_sums(1, 2 * NG - 1, False)



def kernel(x, adj, L0_gnn_h, L1_gnn_W, L1_gnn_b):
    import numpy as np
    import concourse.bacc as bacc
    from concourse.bass_utils import run_bass_kernel_spmd

    x, adj, h, w, b = (np.asarray(a) for a in (x, adj, L0_gnn_h, L1_gnn_W, L1_gnn_b))
    rows = x.shape[0]
    groups = rows // GROUP

    def by_partition(a):
        return np.ascontiguousarray(a.reshape(rows // P, P, P).transpose(1, 0, 2))

    blocks = adj.reshape(groups, GROUP, groups, UNITS, PER_UNIT, P).transpose(0, 2, 3, 5, 4, 1)
    laid = np.empty(blocks.shape, adj.dtype)
    for i in range(groups):
        for p in range(groups):
            laid[i, p] = blocks[i, (i + p) % groups]
    arrays = {
        "adj_blocks": laid.reshape(groups * groups * UNITS, P, PER_UNIT * GROUP),
        "x": by_partition(x),
        "h": by_partition(h),
        "w_t": np.ascontiguousarray(w.T),
        "bias": np.ascontiguousarray(b.reshape(1, P)),
    }
    nc = bacc.Bacc("TRN2", target_bir_lowering=False, num_devices=1)
    args = [nc.dram_tensor(n, a.shape, mybir.dt.from_np(a.dtype), kind="ExternalInput").ap()
            for n, a in arrays.items()]
    shape = (P, rows // P, P)
    out = nc.dram_tensor("out", shape, mybir.dt.float32, kind="ExternalOutput").ap()
    res = nc.dram_tensor("res", shape, mybir.dt.float32, kind="Internal").ap()
    graph_kernel(nc, *args, out, res)
    got = run_bass_kernel_spmd(nc, [arrays], core_ids=[0]).results[0]["out"]
    return np.ascontiguousarray(got.transpose(1, 0, 2)).reshape(rows, P)
```

```python
import concourse.bass as bass
from concourse import mybir
from contextlib import ExitStack

P = 128
GROUP = 1024
CHUNKS = GROUP // P
UNITS = 4
PER_UNIT = CHUNKS // UNITS
BANK = 512
HALVES = GROUP // BANK
FIRST, STRIDE = 6, 3
SPLIT_UNITS = 3
DMA_SCRATCH = 1024
EPS = 1e-5
TINY, HUGE = 1.17549435e-38, 3.4028234e38


def graph_kernel(nc, adj_blocks, x, h, w_t, bias, out, res):
    fp32, fp32r = mybir.dt.float32, mybir.dt.float32r
    ALU = mybir.AluOpType
    ACT = mybir.ActivationFunctionType
    NG = x.shape[1] // CHUNKS
    assert NG % 2 == 0 and STRIDE * STRIDE % NG == 1 and UNITS * PER_UNIT == CHUNKS

    class BlockCount:

        def __init__(self, eng, first):
            self.eng, self.reg = eng, eng.alloc_register("blocks_done")
            eng.reg_mov(self.reg, first)

        def now(self):
            return self.eng.snap(self.reg, min_val=NG, max_val=BLOCKS)

        def step(self):
            self.eng.reg_add(self.reg, self.reg, 1)

    BLOCKS = NG * NG + NG * (NG + 1) // 2
    WHOLE = 2

    def columns(I, p):
        return (I + FIRST + p * STRIDE) % NG

    def fused(I, p):
        return columns(I, p) < I

    def shift(I):
        return NG - 3 if isinstance(I, int) and I == NG - 1 else I

    def b_rows(I, p):
        return (p + shift(I)) % NG

    def counted(k):
        return 1 if k < SPLIT_UNITS - 1 else 1 + UNITS - SPLIT_UNITS

    def address(I, K):
        return I * NG + ((NG - FIRST + K) * STRIDE + I * (NG - STRIDE)) % NG

    with ExitStack() as ctx:
        def sb(name, shape, dt=fp32):
            return ctx.enter_context(nc.sbuf_tensor(name, shape, dt))

        def ps(name, shape):
            return ctx.enter_context(nc.psum_tensor(name, shape, fp32))

        def sem(name):
            return ctx.enter_context(nc.semaphore(name))

        xs = sb("xs", [P, NG * CHUNKS, P])
        g = sb("g", [P, NG * CHUNKS, P])
        raw = sb("raw", [P, UNITS, PER_UNIT, GROUP])
        adj_hi = sb("adj_hi", [P, UNITS, PER_UNIT, GROUP], fp32r)
        adj_lo = sb("adj_lo", [P, UNITS, PER_UNIT, GROUP], fp32r)
        x_hi = sb("x_hi", [P, UNITS, PER_UNIT, P], fp32r)
        x_lo = sb("x_lo", [P, UNITS, PER_UNIT, P], fp32r)
        g_hi = sb("g_hi", [P, UNITS, PER_UNIT, P], fp32r)
        g_lo = sb("g_lo", [P, UNITS, PER_UNIT, P], fp32r)
        sums2 = sb("sums2", [P, NG * GROUP])
        addend_0 = sb("addend_0", [P, CHUNKS, P])
        v_0 = sb("v_0", [P, CHUNKS, P])
        x1 = sb("x1", [P, CHUNKS, P])
        addend = [addend_0[:, :, :], xs[:, 0:CHUNKS, :]]
        v = [v_0[:, :, :], xs[:, CHUNKS:2 * CHUNKS, :]]
        total_t = x1[:, :, :].rearrange("p c f -> p (c f)")
        x1_t = v_0[:, :, :].rearrange("p c f -> p (c f)")
        stats = sb("stats", [P, CHUNKS, 6])
        mean_var = sb("mean_var", [P, CHUNKS, 2])
        squares = sb("squares", [P, 2, CHUNKS])
        newton = sb("newton", [P, 2, CHUNKS])
        roots = sb("roots", [P, 2, CHUNKS])
        shift_by = sb("shift_by", [P, CHUNKS])
        positive = sb("positive", [P, CHUNKS])
        r = sb("r", [P, NG * CHUNKS])
        ident = sb("ident", [P, P])
        weights = sb("weights", [P, P])
        bias_row = sb("bias_row", [P, P])
        zeros = sb("zeros", [P, P], mybir.dt.bfloat16)

        acc1 = ps("acc1", [P, GROUP])
        acc2 = ps("acc2", [P, GROUP])
        accb = ps("accb", [P, GROUP])
        by_turns = [acc1, accb]
        scratch = ps("scratch", [P, CHUNKS, P])

        x_loaded = [sem(f"x_loaded{c}") for c in range(NG)]
        consts_loaded = sem("consts_loaded")
        consts_built = sem("consts_built")
        x_shifted = sem("x_shifted")
        adj_loaded = [sem(f"adj_loaded{k}") for k in range(UNITS)]
        hi_ready = sem("hi_ready")
        lo_ready = sem("lo_ready")
        unit_done = sem("unit_done")
        accb_added = sem("accb_added")
        h_loaded = sem("h_loaded")
        res_loaded = [sem(f"res_loaded{q}") for q in range(2)]
        sums2_cleared = sem("sums2_cleared")
        sums_copied = sem("sums_copied")
        totals_ready = sem("totals_ready")
        sums_transposed = sem("sums_transposed")
        squares_ready = sem("squares_ready")
        roots_ready = sem("roots_ready")
        x1_ready = sem("x1_ready")
        x1_transposed = sem("x1_transposed")
        x1_t_copied = sem("x1_t_copied")
        scales_ready = sem("scales_ready")
        h_ready = sem("h_ready")
        g_ready = sem("g_ready")
        result_ready = sem("result_ready")
        result_stored = sem("result_stored")
        dve_step = sem("dve_step")

        block = ctx.enter_context(nc.Block())

        @block.sync
        def _(sp):
            def load_block(at, b, split=UNITS, whole=0):
                at = at if isinstance(at, int) else sp.snap(at)
                for k in range(UNITS):
                    src = adj_blocks[bass.ds(at, 1), k, :, :].rearrange("o p n -> (o p) n")
                    if k < split:
                        sp.wait_ge(lo_ready, (b - whole) * UNITS + k + 1)
                    else:
                        sp.wait_ge(unit_done, b * UNITS + k + 1)
                    sp.dma_start(raw[:, k, :, :].rearrange("p j i -> p (j i)"), src).then_inc(adj_loaded[k], 16)

            def row_group(I):
                with sp.Fori(0, NG) as p:
                    load_block(I * NG + p, count.now())
                    count.step()
                    with sp.If(p + shift(I) >= NG):
                        load_block(address(b_rows(I, p), I - 1), count.now())
                        count.step()

            with sp.Fori(0, NG) as p:
                load_block(p, p)
            count = BlockCount(sp, NG)
            with sp.Fori(1, NG - 1) as I:
                row_group(I)
            row_group(NG - 1)
            for n in range(2):
                load_block(address(NG - 3 + n, NG - 2), BLOCKS - NG - 2 + n, 0 if n else UNITS)
            load_block(address(0, NG - 1), BLOCKS - NG, 0)
            with sp.Fori(1, NG) as n:
                load_block(address(n, NG - 1), n + (BLOCKS - NG), SPLIT_UNITS, WHOLE)

        def group(n):
            return slice(columns(0, n) * CHUNKS, (columns(0, n) + 1) * CHUNKS)

        @block.gpsimd
        def _(pool):
            pool.memset(ident[:, :], 0.0).then_inc(consts_built, 1)
            pool.memset(zeros[:, :], 0.0).then_inc(consts_built, 1)
            pool.wait_ge(consts_built, 2)
            pool.affine_select(out=ident[:, :], in_=ident[:, :], compare_op=ALU.not_equal, fill=1.0, base=0,
                               pattern=[[-1, P]], channel_multiplier=1).then_inc(consts_built, 1)
            pool.dma_start(xs[:, group(1), :], x[:, group(1), :]).then_inc(x_loaded[1], 16)
            pool.dma_start(weights[:, :], w_t).then_inc(consts_loaded, 16)
            pool.dma_start(bias_row[:, :], bias.to_broadcast([P, P])).then_inc(consts_loaded, 16)
            for n in range(NG):
                if n == 2:
                    pool.memset(sums2[:, :], 0.0).then_inc(sums2_cleared, 1)
                part = xs[:, group(n), :]
                pool.wait_ge(x_loaded[n], 16)
                pool.tensor_tensor(part[:, :, 1:P], part[:, :, 1:P],
                                   part[:, :, 0:1].to_broadcast([P, CHUNKS, P - 1]),
                                   ALU.subtract).then_inc(x_shifted, 1)
                pool.wait_ge(x_shifted, 2 * n + 1)
                pool.memset(part[:, :, 0:1], 1.0).then_inc(x_shifted, 1)
                if n + 2 < NG:
                    pool.wait_ge(unit_done, n * UNITS + 1)
                    pool.dma_start(xs[:, group(n + 2), :], x[:, group(n + 2), :]).then_inc(x_loaded[n + 2], 16)

            def rows(tensor, I):
                return tensor[:, bass.ds(I * CHUNKS, CHUNKS), :]

            def store(tensor, I, q, s):
                pool.wait_ge(result_ready, s + 2)
                pool.dma_start(rows(tensor, I), v[q][:, :, :]).then_inc(result_stored, 16)
                pool.wait_ge(result_stored, s * 16 + 16)

            def load_h(I):
                pool.dma_start(addend[0][:, :, :], rows(h, I)).then_inc(h_loaded, 16)

            def load_res(I, q):
                pool.dma_start(addend[q][:, :, :], rows(res, I)).then_inc(res_loaded[q], 16)

            load_h(0)
            with pool.Fori(0, NG - 1) as I:
                store(res, I, 0, I)
                load_h(I + 1)
            store(res, NG - 1, 0, NG - 1)
            for q in range(2):
                load_res(q, q)
            with pool.Fori(0, NG // 2 - 1) as pair:
                for q in range(2):
                    store(out, pair * 2 + q, q, pair * 2 + (NG + q))
                    load_res(pair * 2 + (q + 2), q)
            for q in range(2):
                store(out, NG - 2 + q, q, 2 * NG - 2 + q)

        @block.scalar
        def _(act):
            act.dma_start(xs[:, group(0), :], x[:, group(0), :]).then_inc(x_loaded[0], 16)
            act.wait_ge(consts_built, 3)
            act.activation(roots[:, :, :], ident[:, 0:2 * CHUNKS].rearrange("p (a c) -> p a c", a=2), ACT.Sqrt)

            def hi_parts(b, k, K, with_x, with_g, parts=1):
                act.wait_ge(unit_done, b * UNITS + k + 1)
                act.wait_ge(adj_loaded[k], b * 16 + 16)
                last = act.activation(adj_hi[:, k, :, :], raw[:, k, :, :], ACT.Copy)
                chunks = bass.ds(K * CHUNKS + k * PER_UNIT, PER_UNIT)

                def g_part():
                    act.wait_ge(g_ready, K + 1)
                    return act.activation(g_hi[:, k, :, :], g[:, chunks, :], ACT.Copy)

                if with_g is True:
                    last = g_part()
                elif with_g is not False:
                    with act.If(with_g):
                        g_part()
                if with_x:
                    last = act.activation(x_hi[:, k, :, :], xs[:, chunks, :], ACT.Copy)
                last.then_inc(hi_ready, parts)

            def copy_sums(b):
                act.wait_ge(unit_done, b * UNITS)
                act.activation(total_t, acc1[:, :], ACT.Copy).then_inc(sums_copied, 1)

            def norm(to, q, s):
                act.wait_ge(scales_ready, s + 1)
                for c in range(CHUNKS):
                    last = act.activation(to(c), v[q][:, c, :], ACT.Identity, bias=shift_by[:, c:c + 1],
                                          scale=roots[:, 1, c:c + 1])
                return last

            def second_norm(n, q):
                norm(lambda c: v[q][:, c, :], q, n + NG).then_inc(result_ready, 1)

            def take_roots(s):
                act.wait_ge(squares_ready, s + 1)
                act.activation(roots[:, :, :], squares[:, :, :], ACT.Sqrt).then_inc(roots_ready, 1)

            def copy_x1_t(s):
                act.wait_ge(x1_transposed, s + 1)
                act.activation(x1_t, scratch[:, :, :], ACT.Copy).then_inc(x1_t_copied, 1)

            def hosted(s, p, k):
                if (p, k) == (0, 3):
                    take_roots(s)
                if (p, k) == (1, 0):
                    norm(lambda c: x1[:, c, :], 0, s).then_inc(x1_ready, 1)
                if (p, k) == (1, 3):
                    copy_x1_t(s)

            def row_group(I):
                for p in range(2):
                    b = count.now()
                    if p == 0:
                        copy_sums(b)
                    for k in range(UNITS):
                        hi_parts(b, k, columns(I, p), True, fused(I, p))
                        hosted(I - 1, p, k)
                    count.step()
                with act.Fori(2, NG) as p:
                    b = count.now()
                    for k in range(UNITS):
                        hi_parts(b, k, columns(I, p), True, fused(I, p))
                    count.step()
                    with act.If(p + shift(I) >= NG):
                        b = count.now()
                        for k in range(UNITS):
                            hi_parts(b, k, I - 1, False, True)
                        count.step()

            def first_row_group(p):
                for k in range(UNITS):
                    act.wait_ge(x_shifted, p * 2 + 2)
                    hi_parts(p, k, columns(0, p), True, False)

            with act.Fori(0, NG) as p:
                first_row_group(p)
            count = BlockCount(act, NG)
            act.wait_ge(unit_done, NG * UNITS + UNITS)
            with act.Fori(1, NG - 1) as I:
                row_group(I)
            row_group(NG - 1)
            for p in range(2):
                b = BLOCKS - NG - 2 + p
                if p == 0:
                    copy_sums(b)
                for k in range(UNITS):
                    hosted(NG - 1, p, k)
            for n in range(2):
                for k in range(SPLIT_UNITS):
                    hi_parts(BLOCKS - NG + n, k, NG - 1, False, n == 0, counted(k))
            with act.Fori(0, NG // 2 - 1) as pair:
                for q in range(2):
                    for k in range(SPLIT_UNITS):
                        hi_parts(pair * 2 + (q + 2 + BLOCKS - NG), k, NG - 1, False, False, counted(k))
                        if k == 0:
                            take_roots(pair * 2 + (q + NG))
                        if k == 1:
                            second_norm(pair * 2 + q, q)
            take_roots(2 * NG - 2)
            second_norm(NG - 2, 0)
            act.wait_ge(result_ready, 2 * NG)
            take_roots(2 * NG - 1)
            second_norm(NG - 1, 1)

        @block.vector
        def _(dve):
            STEPS_A, STEPS_B = 9, 7

            def lo_parts(b, k, K, with_x, with_g, parts=1):
                chunks = bass.ds(K * CHUNKS + k * PER_UNIT, PER_UNIT)
                dve.wait_ge(hi_ready, b * UNITS + k + 1)
                last = dve.tensor_tensor(adj_lo[:, k, :, :], raw[:, k, :, :],
                                         adj_hi[:, k, :, :].bitcast(fp32), ALU.subtract)

                def g_part():
                    return dve.tensor_tensor(g_lo[:, k, :, :], g[:, chunks, :], g_hi[:, k, :, :].bitcast(fp32),
                                             ALU.subtract)

                if with_g is True:
                    last = g_part()
                elif with_g is not False:
                    with dve.If(with_g):
                        g_part()
                if with_x:
                    last = dve.tensor_tensor(x_lo[:, k, :, :], xs[:, chunks, :], x_hi[:, k, :, :].bitcast(fp32),
                                             ALU.subtract)
                last.then_inc(lo_ready, parts)

            def step(instruction, count):
                instruction.then_inc(dve_step, 1)
                dve.wait_ge(dve_step, count)

            def add_sums(b, acc, I):
                dve.wait_ge(unit_done, b * UNITS + UNITS)
                part = sums2[:, bass.ds(I * GROUP, GROUP)]
                return dve.tensor_tensor(part, acc[:, :], part, ALU.add)

            def statistics(q, done, row_sums):
                for c in range(CHUNKS):
                    last = dve.bn_stats(stats[:, c, :], v[q][:, c, :])
                step(last, done + 1)
                row_sums()
                for c in range(CHUNKS):
                    last = dve.bn_aggr(mean_var[:, c, :], stats[:, c, :])
                step(last, done + 2)
                dve.tensor_scalar(squares[:, 1, :], mean_var[:, :, 1], EPS, None, ALU.add).then_inc(squares_ready, 1)

            def scales(s, done):
                dve.wait_ge(roots_ready, s + 1)
                step(dve.reciprocal(roots[:, :, :], roots[:, :, :]), done + 1)
                step(dve.tensor_tensor(newton[:, :, :], squares[:, :, :], roots[:, :, :], ALU.mult), done + 2)
                step(dve.scalar_tensor_tensor(newton[:, :, :], newton[:, :, :], -0.5, roots[:, :, :],
                                              ALU.mult, ALU.mult), done + 3)
                step(dve.scalar_tensor_tensor(roots[:, :, :], newton[:, :, :], 1.5, roots[:, :, :],
                                              ALU.add, ALU.mult), done + 4)
                dve.scalar_tensor_tensor(shift_by[:, :], mean_var[:, :, 0], -1.0, roots[:, 1, :],
                                         ALU.mult, ALU.mult).then_inc(scales_ready, 1)

            def hosted(s, p, k):
                own = bass.ds(s * CHUNKS, CHUNKS)
                done = s * STEPS_A
                if (p, k) == (0, 0):
                    dve.wait_ge(h_loaded, s * 16 + 16)
                    step(dve.scalar_tensor_tensor(v[0][:, :, :], addend[0][:, :, :], 0.1, xs[:, own, :],
                                                  ALU.mult, ALU.add), done + 1)
                if (p, k) == (0, 2):
                    dve.wait_ge(sums_transposed, s + 1)
                    dve.scalar_tensor_tensor(v[0][:, :, 1:P], scratch[:, :, 1:P], 0.9, v[0][:, :, 1:P],
                                             ALU.mult, ALU.add)
                    dve.tensor_scalar(positive[:, :], scratch[:, :, 0], 1.0, 0.0, ALU.add, ALU.is_gt)
                    dve.tensor_scalar(squares[:, 0, :], scratch[:, :, 0], 1.0, TINY, ALU.add, ALU.max)
                    step(dve.tensor_scalar(v[0][:, :, 0], addend[0][:, :, 0], 0.1, None, ALU.mult), done + 2)
                    statistics(0, done + 2, lambda: dve.tensor_scalar(squares[:, 0, :], squares[:, 0, :], HUGE, None,
                                                                      ALU.min))
                if (p, k) == (1, 0):
                    scales(s, done + 4)
                    dve.tensor_tensor(r[:, own], roots[:, 0, :], positive[:, :], ALU.mult)
                if (p, k) == (1, 3):
                    dve.wait_ge(consts_loaded, 32)
                    dve.wait_ge(h_ready, s + 1)
                    step(dve.tensor_tensor(v[0][:, :, :], scratch[:, :, :],
                                           bias_row[:, :].unsqueeze(1).to_broadcast([P, CHUNKS, P]), ALU.add),
                         done + 9)
                    dve.tensor_tensor(g[:, own, :], v[0][:, :, :],
                                      r[:, own].unsqueeze(2).to_broadcast([P, CHUNKS, P]),
                                      ALU.mult).then_inc(g_ready, 1)
                    dve.wait_ge(g_ready, s + 1)
                    for c in range(CHUNKS):
                        at = bass.ds(s * CHUNKS + c, 1)
                        last = dve.scalar_tensor_tensor(v[0][:, c, :], g[:, at, :].rearrange("p o f -> p (o f)"),
                                                        r[:, at], x1[:, c, :], ALU.mult, ALU.add)
                    last.then_inc(result_ready, 1)

            def add_acc2(b, I):
                dve.wait_ge(unit_done, b * UNITS)
                part = sums2[:, bass.ds(I * GROUP, GROUP)]
                dve.tensor_tensor(part, acc2[:, :], part, ALU.add)

            def row_group(I):
                b = count.now()
                if isinstance(I, int):
                    add_acc2(b, I - 1)
                else:
                    with dve.If(I >= 2):
                        add_acc2(b, I - 1)
                for p in range(2):
                    b = count.now()
                    for k in range(UNITS):
                        lo_parts(b, k, columns(I, p), True, fused(I, p))
                        if (p, k) == (0, 3):
                            if isinstance(I, int):
                                add_sums(b, accb, b_rows(I - 1, NG - 1))
                            else:
                                with dve.If(I >= 2):
                                    add_sums(b, accb, (I + (NG - 2)) % NG)
                        hosted(I - 1, p, k)
                    count.step()
                with dve.Fori(2, NG) as p:
                    b = count.now()
                    for k in range(UNITS):
                        lo_parts(b, k, columns(I, p), True, fused(I, p))
                        if k == 3:
                            with dve.If(p + shift(I) >= NG + 1):
                                add_sums(b, accb, b_rows(I, p + (NG - 1)))
                    count.step()
                    with dve.If(p + shift(I) >= NG):
                        b = count.now()
                        for k in range(UNITS):
                            lo_parts(b, k, I - 1, False, True)
                        count.step()

            def complete(b, acc, n):
                dve.wait_ge(unit_done, b * UNITS + UNITS)
                dve.tensor_tensor(total_t, acc[:, :], sums2[:, bass.ds(n * GROUP, GROUP)],
                                  ALU.add).then_inc(totals_ready, 1)

            def second_statistics(n, q, turns):
                dve.wait_ge(res_loaded[q], turns * 16 + 16)
                dve.wait_ge(sums_transposed, n + (NG + 1))
                for c in range(CHUNKS):
                    last = dve.scalar_tensor_tensor(v[q][:, c, :], scratch[:, c, :], r[:, bass.ds(n * CHUNKS + c, 1)],
                                                    addend[q][:, c, :], ALU.mult, ALU.add)
                done = n * STEPS_B + NG * STEPS_A
                step(last, done + 1)
                statistics(q, done + 1, lambda: dve.memset(squares[:, 0, :], 1.0))

            def second_scales(n):
                scales(n + NG, n * STEPS_B + (NG * STEPS_A + 3))

            dve.sem_inc(lo_ready, UNITS)
            dve.sem_inc(result_ready, 1)
            with dve.Fori(0, NG) as p:
                for k in range(UNITS):
                    lo_parts(p, k, columns(0, p), True, False)
            dve.wait_ge(sums2_cleared, 1)
            count = BlockCount(dve, NG)
            with dve.Fori(1, NG - 1) as I:
                row_group(I)
            row_group(NG - 1)
            add_acc2(BLOCKS - NG - 2, NG - 1)
            add_sums(BLOCKS - NG - 2, accb, NG - 4).then_inc(accb_added, 1)
            for p in range(2):
                for k in range(UNITS):
                    hosted(NG - 1, p, k)
            for n in range(2):
                add_sums(BLOCKS - NG - 1 + n, by_turns[n], NG - 3 + n)
                for k in range(SPLIT_UNITS):
                    lo_parts(BLOCKS - NG - WHOLE + n, k, NG - 1, False, n == 0, counted(k))
            complete(BLOCKS - NG + 1, by_turns[0], 0)
            second_statistics(0, 0, 0)
            with dve.Fori(0, NG // 2 - 1) as pair:
                for q in range(2):
                    b = pair * 2 + (q + 2 + BLOCKS - NG)
                    for k in range(SPLIT_UNITS):
                        lo_parts(b - WHOLE, k, NG - 1, False, False, counted(k))
                        if k == 0:
                            second_scales(pair * 2 + q)
                    complete(b, by_turns[1 - q], pair * 2 + (q + 1))
                    second_statistics(pair * 2 + (q + 1), 1 - q, pair + q)
            second_scales(NG - 2)
            complete(BLOCKS, by_turns[1], NG - 1)
            second_statistics(NG - 1, 1, NG // 2 - 1)
            second_scales(NG - 1)

        @block.tensor
        def _(pe):
            def products(to, hi, lo, k, start):
                for half in range(HALVES):
                    cols = slice(half * BANK, (half + 1) * BANK)
                    for j in range(PER_UNIT):
                        fresh = start and k == 0 and j == 0
                        pe.matmul(to[:, cols], lo[:, k, j, :], adj_hi[:, k, j, cols], start=fresh, stop=False,
                                  skip_group_check=True)
                        pe.matmul(to[:, cols], hi[:, k, j, :], adj_hi[:, k, j, cols], start=False, stop=False,
                                  skip_group_check=True)
                        last = pe.matmul(to[:, cols], hi[:, k, j, :], adj_lo[:, k, j, cols],
                                         start=False, stop=True, skip_group_check=True)
                return last

            def unit_a(b, k, start, with_g):
                pe.wait_ge(lo_ready, b * UNITS + (k + 1 + UNITS))
                if with_g is True:
                    products(acc2, g_hi, g_lo, k, False)
                elif with_g is not False:
                    with pe.If(with_g):
                        products(acc2, g_hi, g_lo, k, False)
                products(acc1, x_hi, x_lo, k, start).then_inc(unit_done, 1)

            def whole_unit_b(b, k, K, acc):
                pe.wait_ge(adj_loaded[k], b * 16 + 16)
                for half in range(HALVES):
                    cols = slice(half * BANK, (half + 1) * BANK)
                    for j in range(PER_UNIT):
                        last = pe.matmul(acc[:, cols], g[:, K * CHUNKS + k * PER_UNIT + j, :], raw[:, k, j, cols],
                                         start=k == 0 and j == 0, stop=True, skip_group_check=True)
                last.then_inc(unit_done, 1)

            def unit_b(b, k, acc):
                pe.wait_ge(lo_ready, b * UNITS + (k + 1 + UNITS))
                products(acc, g_hi, g_lo, k, True).then_inc(unit_done, 1)

            def transpose(source):
                for c in range(CHUNKS):
                    last = pe.transpose(scratch[:, c, :], source(c), ident[:, :])
                return last

            def clear_acc2():
                for part in range(GROUP // P):
                    pe.matmul(acc2[:, part * P:(part + 1) * P], zeros[:, :], zeros[:, :],
                              start=part % (BANK // P) == 0, stop=False, skip_group_check=True)

            def hosted(s, p, k):
                if (p, k) == (0, 3):
                    pe.wait_ge(x1_ready, s + 1)
                    transpose(lambda c: x1[:, c, :]).then_inc(x1_transposed, 1)
                if (p, k) == (1, 1):
                    pe.wait_ge(consts_loaded, 32)
                    pe.wait_ge(x1_t_copied, s + 1)
                    for c in range(CHUNKS):
                        last = pe.matmul(scratch[:, c, :], x1_t[:, c * P:(c + 1) * P], weights[:, :],
                                         start=True, stop=True)
                    last.then_inc(h_ready, 1)

            def transpose_sums(s):
                pe.wait_ge(result_ready, s + 1)
                pe.wait_ge(sums_copied, s + 1)
                transpose(lambda c: total_t[:, c * P:(c + 1) * P]).then_inc(sums_transposed, 1)

            def row_group(I):
                transpose_sums(I - 1)
                pe.wait_ge(lo_ready, count.now() * UNITS + (1 + UNITS))
                clear_acc2()
                for p in range(2):
                    b = count.now()
                    for k in range(UNITS):
                        unit_a(b, k, p == 0, fused(I, p))
                        hosted(I - 1, p, k)
                    count.step()
                with pe.Fori(2, NG) as p:
                    b = count.now()
                    for k in range(UNITS):
                        unit_a(b, k, False, fused(I, p))
                    count.step()
                    with pe.If(p + shift(I) >= NG):
                        b = count.now()
                        for k in range(UNITS):
                            unit_b(b, k, accb)
                        count.step()

            def transpose_totals(n):
                pe.wait_ge(totals_ready, n + 1)
                transpose(lambda c: total_t[:, c * P:(c + 1) * P]).then_inc(sums_transposed, 1)

            pe.sem_inc(unit_done, UNITS)
            pe.wait_ge(consts_built, 3)
            for k in range(UNITS):
                unit_a(0, k, True, False)
            with pe.Fori(1, NG) as p:
                for k in range(UNITS):
                    unit_a(p, k, False, False)
            count = BlockCount(pe, NG)
            with pe.Fori(1, NG - 1) as I:
                row_group(I)
            row_group(NG - 1)
            transpose_sums(NG - 1)
            for p in range(2):
                if p == 1:
                    pe.wait_ge(accb_added, 1)
                for k in range(UNITS):
                    whole_unit_b(BLOCKS - NG - 2 + p, k, NG - 2, by_turns[p])
                    hosted(NG - 1, p, k)
            pe.wait_ge(g_ready, NG)

            def last_block(b, q, n):
                for k in range(UNITS):
                    if k < SPLIT_UNITS:
                        unit_b(b - WHOLE, k, by_turns[q])
                    else:
                        whole_unit_b(b, k, NG - 1, by_turns[q])
                    if k == 1 and n is not None:
                        transpose_totals(n)

            last_block(BLOCKS - NG, 0, None)
            last_block(BLOCKS - NG + 1, 1, 0)
            with pe.Fori(0, NG // 2 - 1) as pair:
                for q in range(2):
                    last_block(pair * 2 + (q + 2 + BLOCKS - NG), q, pair * 2 + (q + 1))
            transpose_totals(NG - 1)



def kernel(x, adj, L0_gnn_h, L1_gnn_W, L1_gnn_b):
    import numpy as np
    import concourse.bacc as bacc
    from concourse.bass_utils import run_bass_kernel_spmd

    x, adj, h, w, b = (np.asarray(a) for a in (x, adj, L0_gnn_h, L1_gnn_W, L1_gnn_b))
    rows = x.shape[0]
    groups = rows // GROUP

    def by_partition(a):
        return np.ascontiguousarray(a.reshape(rows // P, P, P).transpose(1, 0, 2))

    blocks = adj.reshape(groups, GROUP, groups, UNITS, PER_UNIT, P).transpose(0, 2, 3, 5, 4, 1)
    laid = np.empty(blocks.shape, adj.dtype)
    for i in range(groups):
        for p in range(groups):
            laid[i, p] = blocks[i, (i + FIRST + p * STRIDE) % groups]
    arrays = {
        "adj_blocks": laid.reshape(groups * groups, UNITS, P, PER_UNIT * GROUP),
        "x": by_partition(x),
        "h": by_partition(h),
        "w_t": np.ascontiguousarray(w.T),
        "bias": np.ascontiguousarray(b.reshape(1, P)),
    }
    nc = bacc.Bacc("TRN2", target_bir_lowering=False, num_devices=1,
                   dynamic_dma_scratch_size=DMA_SCRATCH)
    args = [nc.dram_tensor(n, a.shape, mybir.dt.from_np(a.dtype), kind="ExternalInput").ap()
            for n, a in arrays.items()]
    shape = (P, rows // P, P)
    out = nc.dram_tensor("out", shape, mybir.dt.float32, kind="ExternalOutput").ap()
    res = nc.dram_tensor("res", shape, mybir.dt.float32, kind="Internal").ap()
    graph_kernel(nc, *args, out, res)
    got = run_bass_kernel_spmd(nc, [arrays], core_ids=[0]).results[0]["out"]
    return np.ascontiguousarray(got.transpose(1, 0, 2)).reshape(rows, P)
```

```python
import concourse.bass as bass
from concourse import mybir
from contextlib import ExitStack

P = 128
GROUP = 1024
CHUNKS = GROUP // P
UNITS = 4
PER_UNIT = CHUNKS // UNITS
BANK = 512
HALVES = GROUP // BANK
FIRST, STRIDE = 6, 3
SPLIT_UNITS = 2
DMA_SCRATCH = 1024
EPS = 1e-5
TINY, HUGE = 1.17549435e-38, 3.4028234e38


def graph_kernel(nc, adj_blocks, x, h, w_t, bias, out, res):
    fp32, fp32r = mybir.dt.float32, mybir.dt.float32r
    ALU = mybir.AluOpType
    ACT = mybir.ActivationFunctionType
    NG = x.shape[1] // CHUNKS
    assert NG % 2 == 0 and STRIDE * STRIDE % NG == 1 and UNITS * PER_UNIT == CHUNKS

    class BlockCount:

        def __init__(self, eng, first):
            self.eng, self.reg = eng, eng.alloc_register("blocks_done")
            eng.reg_mov(self.reg, first)

        def now(self):
            return self.eng.snap(self.reg, min_val=NG, max_val=BLOCKS)

        def step(self):
            self.eng.reg_add(self.reg, self.reg, 1)

    BLOCKS = NG * NG + NG * (NG + 1) // 2
    WHOLE = 1

    def columns(I, p):
        return (I + FIRST + p * STRIDE) % NG

    def fused(I, p):
        return columns(I, p) < I

    def shift(I):
        return NG - 3 if isinstance(I, int) and I == NG - 1 else I

    def b_rows(I, p):
        return (p + shift(I)) % NG

    def counted(k):
        return 1 if k < SPLIT_UNITS - 1 else 1 + UNITS - SPLIT_UNITS

    def chunk(tensor, I, c):
        return tensor[:, bass.ds(I * CHUNKS + c, 1), :].rearrange("p o f -> p (o f)")

    def address(I, K):
        return I * NG + ((NG - FIRST + K) * STRIDE + I * (NG - STRIDE)) % NG

    with ExitStack() as ctx:
        def sb(name, shape, dt=fp32):
            return ctx.enter_context(nc.sbuf_tensor(name, shape, dt))

        def ps(name, shape):
            return ctx.enter_context(nc.psum_tensor(name, shape, fp32))

        def sem(name):
            return ctx.enter_context(nc.semaphore(name))

        xs = sb("xs", [P, NG * CHUNKS, P])
        g = sb("g", [P, NG * CHUNKS, P])
        raw = sb("raw", [P, UNITS, PER_UNIT, GROUP])
        adj_hi = sb("adj_hi", [P, UNITS, PER_UNIT, GROUP], fp32r)
        adj_lo = sb("adj_lo", [P, UNITS, PER_UNIT, GROUP], fp32r)
        x_hi = sb("x_hi", [P, UNITS, PER_UNIT, P], fp32r)
        x_lo = sb("x_lo", [P, UNITS, PER_UNIT, P], fp32r)
        g_hi = sb("g_hi", [P, UNITS, PER_UNIT, P], fp32r)
        g_lo = sb("g_lo", [P, UNITS, PER_UNIT, P], fp32r)
        sums2 = sb("sums2", [P, NG * GROUP])
        h_rows = sb("h_rows", [P, CHUNKS, P])
        v = sb("v", [P, CHUNKS, P])
        x1 = sb("x1", [P, CHUNKS, P])
        res_sb = xs
        sum_rows = [v, h_rows]
        total_t = x1[:, :, :].rearrange("p c f -> p (c f)")
        x1_t = v[:, :, :].rearrange("p c f -> p (c f)")
        stats = sb("stats", [P, CHUNKS, 6])
        mean_var = sb("mean_var", [P, CHUNKS, 2])
        squares = sb("squares", [P, 2, CHUNKS])
        newton = sb("newton", [P, 2, CHUNKS])
        roots = sb("roots", [P, 2, CHUNKS])
        shift_by = sb("shift_by", [P, CHUNKS])
        positive = sb("positive", [P, CHUNKS])
        r = sb("r", [P, NG * CHUNKS])
        ident = sb("ident", [P, P])
        weights = sb("weights", [P, P])
        bias_row = sb("bias_row", [P, P])
        zeros = sb("zeros", [P, P], mybir.dt.bfloat16)

        acc1 = ps("acc1", [P, GROUP])
        acc2 = ps("acc2", [P, GROUP])
        accb = ps("accb", [P, GROUP])
        by_turns = [acc1, accb]
        scratch = ps("scratch", [P, CHUNKS, P])

        x_loaded = [sem(f"x_loaded{c}") for c in range(NG)]
        consts_loaded = sem("consts_loaded")
        consts_built = sem("consts_built")
        x_shifted = sem("x_shifted")
        adj_loaded = [sem(f"adj_loaded{k}") for k in range(UNITS)]
        hi_ready = sem("hi_ready")
        lo_ready = sem("lo_ready")
        unit_done = sem("unit_done")
        h_loaded = sem("h_loaded")
        res_loaded = sem("res_loaded")
        sums2_cleared = sem("sums2_cleared")
        sums_copied = sem("sums_copied")
        totals_ready = sem("totals_ready")
        sums_transposed = sem("sums_transposed")
        squares_ready = sem("squares_ready")
        roots_ready = sem("roots_ready")
        x1_ready = sem("x1_ready")
        x1_transposed = sem("x1_transposed")
        x1_t_copied = sem("x1_t_copied")
        scales_ready = sem("scales_ready")
        h_ready = sem("h_ready")
        g_ready = sem("g_ready")
        result_ready = sem("result_ready")
        result_stored = sem("result_stored")
        end_ready = sem("end_ready")
        end_stored = sem("end_stored")
        dve_step = sem("dve_step")

        block = ctx.enter_context(nc.Block())

        @block.sync
        def _(sp):
            def load_block(at, b, split=UNITS, whole=0):
                at = at if isinstance(at, int) else sp.snap(at)
                for k in range(UNITS):
                    src = adj_blocks[bass.ds(at, 1), k, :, :].rearrange("o p n -> (o p) n")
                    if k < split:
                        sp.wait_ge(lo_ready, (b - whole) * UNITS + k + 1)
                    else:
                        sp.wait_ge(unit_done, b * UNITS + k + 1)
                    sp.dma_start(raw[:, k, :, :].rearrange("p j i -> p (j i)"), src).then_inc(adj_loaded[k], 16)

            def row_group(I):
                with sp.Fori(0, NG) as p:
                    load_block(I * NG + p, count.now())
                    count.step()
                    with sp.If(p + shift(I) >= NG):
                        load_block(address(b_rows(I, p), I - 1), count.now())
                        count.step()

            with sp.Fori(0, NG) as p:
                load_block(p, p)
            count = BlockCount(sp, NG)
            with sp.Fori(1, NG - 1) as I:
                row_group(I)
            row_group(NG - 1)
            load_block(address(NG - 3, NG - 2), BLOCKS - NG - 2)
            load_block(address(NG - 2, NG - 2), BLOCKS - NG - 1, 0)
            load_block(address(0, NG - 1), BLOCKS - NG, UNITS, WHOLE)
            with sp.Fori(1, NG) as n:
                load_block(address(n, NG - 1), n + (BLOCKS - NG), SPLIT_UNITS, WHOLE)

            middle, end = NG * CHUNKS - CHUNKS // 2, NG * CHUNKS
            sp.wait_ge(result_ready, 2 * NG + 1)
            sp.dma_start(out[:, middle - CHUNKS // 2:middle, :],
                         res_sb[:, middle - CHUNKS // 2:middle, :]).then_inc(end_stored, 16)
            sp.wait_ge(end_ready, 1)
            sp.dma_start(out[:, middle:end, :], res_sb[:, middle:end, :]).then_inc(end_stored, 16)
            sp.wait_ge(end_stored, 32)

        def group(n):
            return slice(columns(0, n) * CHUNKS, (columns(0, n) + 1) * CHUNKS)

        @block.gpsimd
        def _(pool):
            pool.memset(ident[:, :], 0.0).then_inc(consts_built, 1)
            pool.memset(zeros[:, :], 0.0).then_inc(consts_built, 1)
            pool.wait_ge(consts_built, 2)
            pool.affine_select(out=ident[:, :], in_=ident[:, :], compare_op=ALU.not_equal, fill=1.0, base=0,
                               pattern=[[-1, P]], channel_multiplier=1).then_inc(consts_built, 1)
            pool.dma_start(xs[:, group(1), :], x[:, group(1), :]).then_inc(x_loaded[1], 16)
            pool.dma_start(weights[:, :], w_t).then_inc(consts_loaded, 16)
            pool.dma_start(bias_row[:, :], bias.to_broadcast([P, P])).then_inc(consts_loaded, 16)
            for n in range(NG):
                if n == 2:
                    pool.memset(sums2[:, :], 0.0).then_inc(sums2_cleared, 1)
                part = xs[:, group(n), :]
                pool.wait_ge(x_loaded[n], 16)
                pool.tensor_tensor(part[:, :, 1:P], part[:, :, 1:P],
                                   part[:, :, 0:1].to_broadcast([P, CHUNKS, P - 1]),
                                   ALU.subtract).then_inc(x_shifted, 1)
                pool.wait_ge(x_shifted, 2 * n + 1)
                pool.memset(part[:, :, 0:1], 1.0).then_inc(x_shifted, 1)
                if n + 2 < NG:
                    pool.wait_ge(unit_done, n * UNITS + 1)
                    pool.dma_start(xs[:, group(n + 2), :], x[:, group(n + 2), :]).then_inc(x_loaded[n + 2], 16)

            def rows(tensor, I):
                return tensor[:, bass.ds(I * CHUNKS, CHUNKS), :]

            def load_h(I):
                pool.dma_start(h_rows[:, :, :], rows(h, I)).then_inc(h_loaded, 16)

            load_h(0)
            with pool.Fori(0, NG - 1) as I:
                pool.wait_ge(result_ready, I + 2)
                pool.dma_start(rows(res, I), v[:, :, :]).then_inc(result_stored, 16)
                pool.wait_ge(result_stored, I * 16 + 16)
                load_h(I + 1)
            for p in range(NG):
                if columns(NG - 1, p) < NG - 1:
                    first = BLOCKS - NG - 2 - (NG + shift(NG - 1))
                    block_a = first + p + max(0, p - (NG - shift(NG - 1)))
                    pool.wait_ge(unit_done, (block_a + 1) * UNITS + UNITS)
                    pool.dma_start(rows(res_sb, columns(NG - 1, p)),
                                   rows(res, columns(NG - 1, p))).then_inc(res_loaded, 16)
            with pool.Fori(0, NG - 1) as n:
                pool.wait_ge(result_ready, n + (NG + 2))
                pool.dma_start(rows(out, n), rows(res_sb, n)).then_inc(result_stored, 16)
            pool.wait_ge(result_stored, (2 * NG - 2) * 16)

        @block.scalar
        def _(act):
            act.dma_start(xs[:, group(0), :], x[:, group(0), :]).then_inc(x_loaded[0], 16)
            act.wait_ge(consts_built, 3)
            act.activation(roots[:, :, :], ident[:, 0:2 * CHUNKS].rearrange("p (a c) -> p a c", a=2), ACT.Sqrt)

            def hi_parts(b, k, K, with_x, with_g, parts=1):
                act.wait_ge(unit_done, b * UNITS + k + 1)
                act.wait_ge(adj_loaded[k], b * 16 + 16)
                last = act.activation(adj_hi[:, k, :, :], raw[:, k, :, :], ACT.Copy)
                chunks = bass.ds(K * CHUNKS + k * PER_UNIT, PER_UNIT)

                def g_part():
                    act.wait_ge(g_ready, K + 1)
                    return act.activation(g_hi[:, k, :, :], g[:, chunks, :], ACT.Copy)

                if with_g is True:
                    last = g_part()
                elif with_g is not False:
                    with act.If(with_g):
                        g_part()
                if with_x:
                    last = act.activation(x_hi[:, k, :, :], xs[:, chunks, :], ACT.Copy)
                last.then_inc(hi_ready, parts)

            def copy_sums(b):
                act.wait_ge(unit_done, b * UNITS)
                act.activation(total_t, acc1[:, :], ACT.Copy).then_inc(sums_copied, 1)

            def norm(to, source, s, chunks=CHUNKS):
                act.wait_ge(scales_ready, s + 1)
                for c in range(chunks):
                    last = act.activation(to(c), source(c), ACT.Identity, bias=shift_by[:, c:c + 1],
                                          scale=roots[:, 1, c:c + 1])
                return last

            def first_norm(s):
                norm(lambda c: x1[:, c, :], lambda c: v[:, c, :], s).then_inc(x1_ready, 1)

            def second_roots(n):
                act.wait_ge(result_ready, n + (NG + 1))
                take_roots(n + NG)

            def second_norm(n, q, chunks=CHUNKS):
                norm(lambda c: chunk(res_sb, n, c), lambda c: sum_rows[q][:, c, :], n + NG,
                     chunks).then_inc(result_ready, 1)

            def take_roots(s):
                act.wait_ge(squares_ready, s + 1)
                act.activation(roots[:, :, :], squares[:, :, :], ACT.Sqrt).then_inc(roots_ready, 1)

            def copy_x1_t(s):
                act.wait_ge(x1_transposed, s + 1)
                act.activation(x1_t, scratch[:, :, :], ACT.Copy).then_inc(x1_t_copied, 1)

            def hosted(s, p, k):
                if (p, k) == (0, 3):
                    take_roots(s)
                if (p, k) == (1, 1):
                    first_norm(s)
                if (p, k) == (1, 3):
                    copy_x1_t(s)

            def row_group(I):
                for p in range(2):
                    b = count.now()
                    for k in range(UNITS):
                        if (p, k) == (0, 0):
                            if isinstance(I, int):
                                copy_sums(b)
                            else:
                                with act.If(I >= 2):
                                    copy_sums(b)
                        hi_parts(b, k, columns(I, p), True, fused(I, p))
                        if (p, k) == (0, 2) and not isinstance(I, int):
                            with act.If(I < 2):
                                copy_sums(NG + 1)
                        hosted(I - 1, p, k)
                    count.step()
                with act.Fori(2, NG) as p:
                    b = count.now()
                    for k in range(UNITS):
                        hi_parts(b, k, columns(I, p), True, fused(I, p))
                    count.step()
                    with act.If(p + shift(I) >= NG):
                        b = count.now()
                        for k in range(UNITS):
                            hi_parts(b, k, I - 1, False, True)
                        count.step()

            def first_row_group(p):
                for k in range(UNITS):
                    act.wait_ge(x_shifted, p * 2 + 2)
                    hi_parts(p, k, columns(0, p), True, False)

            with act.Fori(0, NG) as p:
                first_row_group(p)
            count = BlockCount(act, NG)
            with act.Fori(1, NG - 1) as I:
                row_group(I)
            row_group(NG - 1)
            copy_sums(BLOCKS - NG - 2)
            take_roots(NG - 1)
            first_norm(NG - 1)
            for k in range(UNITS):
                hi_parts(BLOCKS - NG - 1, k, NG - 2, False, True)
                if k == 1:
                    copy_x1_t(NG - 1)
            for n in range(2):
                for k in range(SPLIT_UNITS):
                    hi_parts(BLOCKS - NG + n, k, NG - 1, False, n == 0, counted(k))
            with act.Fori(0, NG // 2 - 1) as pair:
                for q in range(2):
                    for k in range(SPLIT_UNITS):
                        hi_parts(pair * 2 + (q + 2 + BLOCKS - NG), k, NG - 1, False, False, counted(k))
                        if k == 0:
                            second_roots(pair * 2 + q)
                    second_norm(pair * 2 + q, q)
            second_roots(NG - 2)
            second_norm(NG - 2, 0)
            second_roots(NG - 1)
            second_norm(NG - 1, 1, CHUNKS // 2)

        @block.vector
        def _(dve):
            STEPS_A, STEPS_B = 9, 7

            def lo_parts(b, k, K, with_x, with_g, parts=1):
                chunks = bass.ds(K * CHUNKS + k * PER_UNIT, PER_UNIT)
                dve.wait_ge(hi_ready, b * UNITS + k + 1)
                last = dve.tensor_tensor(adj_lo[:, k, :, :], raw[:, k, :, :],
                                         adj_hi[:, k, :, :].bitcast(fp32), ALU.subtract)

                def g_part():
                    return dve.tensor_tensor(g_lo[:, k, :, :], g[:, chunks, :], g_hi[:, k, :, :].bitcast(fp32),
                                             ALU.subtract)

                if with_g is True:
                    last = g_part()
                elif with_g is not False:
                    with dve.If(with_g):
                        g_part()
                if with_x:
                    last = dve.tensor_tensor(x_lo[:, k, :, :], xs[:, chunks, :], x_hi[:, k, :, :].bitcast(fp32),
                                             ALU.subtract)
                last.then_inc(lo_ready, parts)

            def step(instruction, count):
                instruction.then_inc(dve_step, 1)
                dve.wait_ge(dve_step, count)

            def add_sums(b, acc, I):
                dve.wait_ge(unit_done, b * UNITS + UNITS)
                part = sums2[:, bass.ds(I * GROUP, GROUP)]
                return dve.tensor_tensor(part, acc[:, :], part, ALU.add)

            def statistics(source, done, row_sums):
                for c in range(CHUNKS):
                    last = dve.bn_stats(stats[:, c, :], source(c))
                step(last, done + 1)
                row_sums()
                for c in range(CHUNKS):
                    last = dve.bn_aggr(mean_var[:, c, :], stats[:, c, :])
                step(last, done + 2)
                dve.tensor_scalar(squares[:, 1, :], mean_var[:, :, 1], EPS, None, ALU.add).then_inc(squares_ready, 1)

            def scales(s, done):
                dve.wait_ge(roots_ready, s + 1)
                step(dve.reciprocal(roots[:, :, :], roots[:, :, :]), done + 1)
                step(dve.tensor_tensor(newton[:, :, :], squares[:, :, :], roots[:, :, :], ALU.mult), done + 2)
                step(dve.scalar_tensor_tensor(newton[:, :, :], newton[:, :, :], -0.5, roots[:, :, :],
                                              ALU.mult, ALU.mult), done + 3)
                step(dve.scalar_tensor_tensor(roots[:, :, :], newton[:, :, :], 1.5, roots[:, :, :],
                                              ALU.add, ALU.mult), done + 4)
                dve.scalar_tensor_tensor(shift_by[:, :], mean_var[:, :, 0], -1.0, roots[:, 1, :],
                                         ALU.mult, ALU.mult).then_inc(scales_ready, 1)

            def hosted(s, p, k):
                own = bass.ds(s * CHUNKS, CHUNKS)
                done = s * STEPS_A
                if (p, k) == (0, 0):
                    dve.wait_ge(h_loaded, s * 16 + 16)
                    step(dve.scalar_tensor_tensor(v[:, :, :], h_rows[:, :, :], 0.1, xs[:, own, :],
                                                  ALU.mult, ALU.add), done + 1)
                if (p, k) == (0, 2):
                    dve.wait_ge(sums_transposed, s + 1)
                    dve.scalar_tensor_tensor(v[:, :, 1:P], scratch[:, :, 1:P], 0.9, v[:, :, 1:P],
                                             ALU.mult, ALU.add)
                    dve.tensor_scalar(positive[:, :], scratch[:, :, 0], 1.0, 0.0, ALU.add, ALU.is_gt)
                    dve.tensor_scalar(squares[:, 0, :], scratch[:, :, 0], 1.0, TINY, ALU.add, ALU.max)
                    step(dve.tensor_scalar(v[:, :, 0], h_rows[:, :, 0], 0.1, None, ALU.mult), done + 2)
                    statistics(lambda c: v[:, c, :], done + 2,
                               lambda: dve.tensor_scalar(squares[:, 0, :], squares[:, 0, :], HUGE, None, ALU.min))
                if (p, k) == (0, 3):
                    scales(s, done + 4)
                    dve.tensor_tensor(r[:, own], roots[:, 0, :], positive[:, :], ALU.mult)
                if (p, k) == (1, 3):
                    make_g(s)

            def make_g(s):
                own = bass.ds(s * CHUNKS, CHUNKS)
                dve.wait_ge(consts_loaded, 32)
                dve.wait_ge(h_ready, s + 1)
                step(dve.tensor_tensor(v[:, :, :], scratch[:, :, :],
                                       bias_row[:, :].unsqueeze(1).to_broadcast([P, CHUNKS, P]), ALU.add),
                     s * STEPS_A + 9)
                dve.tensor_tensor(g[:, own, :], v[:, :, :],
                                  r[:, own].unsqueeze(2).to_broadcast([P, CHUNKS, P]),
                                  ALU.mult).then_inc(g_ready, 1)

            def make_res(s):
                dve.wait_ge(g_ready, s + 1)
                for c in range(CHUNKS):
                    last_group = isinstance(s, int) and s == NG - 1
                    to = chunk(res_sb, s, c) if last_group else v[:, c, :]
                    last = dve.scalar_tensor_tensor(to, chunk(g, s, c), r[:, bass.ds(s * CHUNKS + c, 1)],
                                                    x1[:, c, :], ALU.mult, ALU.add)
                last.then_inc(result_ready, 1)

            def add_acc2(b, I):
                dve.wait_ge(unit_done, b * UNITS)
                part = sums2[:, bass.ds(I * GROUP, GROUP)]
                dve.tensor_tensor(part, acc2[:, :], part, ALU.add)

            def row_group(I):
                b = count.now()
                if isinstance(I, int):
                    add_acc2(b, I - 1)
                else:
                    with dve.If(I >= 2):
                        add_acc2(b, I - 1)
                for p in range(2):
                    b = count.now()
                    for k in range(UNITS):
                        lo_parts(b, k, columns(I, p), True, fused(I, p))
                        if (p, k) == (0, 3):
                            if isinstance(I, int):
                                add_sums(b, accb, b_rows(I - 1, NG - 1))
                            else:
                                with dve.If(I >= 2):
                                    add_sums(b, accb, (I + (NG - 2)) % NG)
                        hosted(I - 1, p, k)
                    count.step()
                with dve.Fori(2, NG) as p:
                    b = count.now()
                    for k in range(UNITS):
                        lo_parts(b, k, columns(I, p), True, fused(I, p))
                        if k == 1:
                            with dve.If(p == 3):
                                make_res(I - 1)
                        if k == 3:
                            with dve.If(p + shift(I) >= NG + 1):
                                add_sums(b, accb, b_rows(I, p + (NG - 1)))
                    count.step()
                    with dve.If(p + shift(I) >= NG):
                        b = count.now()
                        for k in range(UNITS):
                            lo_parts(b, k, I - 1, False, True)
                        count.step()

            def complete(b, acc, n):
                dve.wait_ge(unit_done, b * UNITS + UNITS)
                dve.tensor_tensor(total_t, acc[:, :], sums2[:, bass.ds(n * GROUP, GROUP)],
                                  ALU.add).then_inc(totals_ready, 1)

            def second_statistics(n, q):
                dve.wait_ge(sums_transposed, n + (NG + 1))
                if not isinstance(n, int):
                    dve.wait_ge(result_ready, n + NG)
                for c in range(CHUNKS):
                    last = dve.scalar_tensor_tensor(sum_rows[q][:, c, :], scratch[:, c, :],
                                                    r[:, bass.ds(n * CHUNKS + c, 1)], chunk(res_sb, n, c),
                                                    ALU.mult, ALU.add)
                done = n * STEPS_B + NG * STEPS_A
                step(last, done + 1)
                statistics(lambda c: sum_rows[q][:, c, :], done + 1, lambda: dve.memset(squares[:, 0, :], 1.0))

            def second_scales(n):
                scales(n + NG, n * STEPS_B + (NG * STEPS_A + 3))

            dve.sem_inc(lo_ready, UNITS)
            dve.sem_inc(result_ready, 1)
            with dve.Fori(0, NG) as p:
                for k in range(UNITS):
                    lo_parts(p, k, columns(0, p), True, False)
            dve.wait_ge(sums2_cleared, 1)
            count = BlockCount(dve, NG)
            with dve.Fori(1, NG - 1) as I:
                row_group(I)
            row_group(NG - 1)
            add_acc2(BLOCKS - NG - 2, NG - 1)
            for k in range(UNITS):
                hosted(NG - 1, 0, k)
            add_sums(BLOCKS - NG - 2, accb, NG - 4)
            for k in range(UNITS):
                lo_parts(BLOCKS - NG - 1 - WHOLE, k, NG - 2, False, True)
                if k == 1:
                    add_sums(BLOCKS - NG - 1, acc1, NG - 3)
                if k == 2:
                    make_g(NG - 1)
            for n in range(2):
                for k in range(SPLIT_UNITS):
                    lo_parts(BLOCKS - NG - WHOLE + n, k, NG - 1, False, n == 0, counted(k))
                if n == 0:
                    add_sums(BLOCKS - NG, acc2, NG - 2)
                    make_res(NG - 1)
                    dve.wait_ge(result_ready, NG + 1)
            dve.wait_ge(res_loaded, (NG - 1) * 16)
            complete(BLOCKS - NG + 1, by_turns[0], 0)
            second_statistics(0, 0)
            with dve.Fori(0, NG // 2 - 1) as pair:
                for q in range(2):
                    b = pair * 2 + (q + 2 + BLOCKS - NG)
                    for k in range(SPLIT_UNITS):
                        lo_parts(b - WHOLE, k, NG - 1, False, False, counted(k))
                        if k == 0:
                            second_scales(pair * 2 + q)
                        if k == SPLIT_UNITS - 2:
                            complete(b, by_turns[1 - q], pair * 2 + (q + 1))
                    second_statistics(pair * 2 + (q + 1), 1 - q)
            second_scales(NG - 2)
            complete(BLOCKS, by_turns[1], NG - 1)
            second_statistics(NG - 1, 1)
            second_scales(NG - 1)
            for c in range(CHUNKS // 2, CHUNKS):
                last = dve.tensor_scalar(chunk(res_sb, NG - 1, c), sum_rows[1][:, c, :], mean_var[:, c, 0:1],
                                         roots[:, 1, c:c + 1], ALU.subtract, ALU.mult)
            last.then_inc(end_ready, 1)

        @block.tensor
        def _(pe):
            def products(to, hi, lo, k, start):
                for half in range(HALVES):
                    cols = slice(half * BANK, (half + 1) * BANK)
                    for j in range(PER_UNIT):
                        fresh = start and k == 0 and j == 0
                        pe.matmul(to[:, cols], lo[:, k, j, :], adj_hi[:, k, j, cols], start=fresh, stop=False,
                                  skip_group_check=True)
                        pe.matmul(to[:, cols], hi[:, k, j, :], adj_hi[:, k, j, cols], start=False, stop=False,
                                  skip_group_check=True)
                        last = pe.matmul(to[:, cols], hi[:, k, j, :], adj_lo[:, k, j, cols],
                                         start=False, stop=True, skip_group_check=True)
                return last

            def unit_a(b, k, start, with_g):
                pe.wait_ge(lo_ready, b * UNITS + (k + 1 + UNITS))
                if with_g is True:
                    products(acc2, g_hi, g_lo, k, False)
                elif with_g is not False:
                    with pe.If(with_g):
                        products(acc2, g_hi, g_lo, k, False)
                products(acc1, x_hi, x_lo, k, start).then_inc(unit_done, 1)

            def whole_unit_b(b, k, K, acc):
                pe.wait_ge(adj_loaded[k], b * 16 + 16)
                for half in range(HALVES):
                    cols = slice(half * BANK, (half + 1) * BANK)
                    for j in range(PER_UNIT):
                        last = pe.matmul(acc[:, cols], g[:, K * CHUNKS + k * PER_UNIT + j, :], raw[:, k, j, cols],
                                         start=k == 0 and j == 0, stop=True, skip_group_check=True)
                last.then_inc(unit_done, 1)

            def unit_b(b, k, acc):
                pe.wait_ge(lo_ready, b * UNITS + (k + 1 + UNITS))
                products(acc, g_hi, g_lo, k, True).then_inc(unit_done, 1)

            def transpose(source):
                for c in range(CHUNKS):
                    last = pe.transpose(scratch[:, c, :], source(c), ident[:, :])
                return last

            def clear_acc2():
                for part in range(GROUP // P):
                    pe.matmul(acc2[:, part * P:(part + 1) * P], zeros[:, :], zeros[:, :],
                              start=part % (BANK // P) == 0, stop=False, skip_group_check=True)

            def hosted(s, p, k):
                if (p, k) == (0, 3):
                    pe.wait_ge(x1_ready, s + 1)
                    transpose(lambda c: x1[:, c, :]).then_inc(x1_transposed, 1)
                if (p, k) == (1, 1):
                    pe.wait_ge(consts_loaded, 32)
                    pe.wait_ge(x1_t_copied, s + 1)
                    for c in range(CHUNKS):
                        last = pe.matmul(scratch[:, c, :], x1_t[:, c * P:(c + 1) * P], weights[:, :],
                                         start=True, stop=True)
                    last.then_inc(h_ready, 1)

            def transpose_sums(s):
                pe.wait_ge(result_ready, s + 1)
                pe.wait_ge(sums_copied, s + 1)
                transpose(lambda c: total_t[:, c * P:(c + 1) * P]).then_inc(sums_transposed, 1)

            def row_group(I):
                transpose_sums(I - 1)
                pe.wait_ge(lo_ready, count.now() * UNITS + (1 + UNITS))
                clear_acc2()
                for p in range(2):
                    b = count.now()
                    for k in range(UNITS):
                        unit_a(b, k, p == 0, fused(I, p))
                        hosted(I - 1, p, k)
                    count.step()
                with pe.Fori(2, NG) as p:
                    b = count.now()
                    for k in range(UNITS):
                        unit_a(b, k, False, fused(I, p))
                    count.step()
                    with pe.If(p + shift(I) >= NG):
                        b = count.now()
                        for k in range(UNITS):
                            unit_b(b, k, accb)
                        count.step()

            def transpose_totals(n):
                pe.wait_ge(totals_ready, n + 1)
                transpose(lambda c: total_t[:, c * P:(c + 1) * P]).then_inc(sums_transposed, 1)

            pe.sem_inc(unit_done, UNITS)
            pe.wait_ge(consts_built, 3)
            for k in range(UNITS):
                unit_a(0, k, True, False)
            with pe.Fori(1, NG) as p:
                for k in range(UNITS):
                    unit_a(p, k, False, False)
            count = BlockCount(pe, NG)
            with pe.Fori(1, NG - 1) as I:
                row_group(I)
            row_group(NG - 1)
            transpose_sums(NG - 1)
            for k in range(UNITS):
                whole_unit_b(BLOCKS - NG - 2, k, NG - 2, acc1)
                hosted(NG - 1, 0, k)
            for k in range(UNITS):
                unit_b(BLOCKS - NG - 1 - WHOLE, k, acc2)
                if k == 0:
                    hosted(NG - 1, 1, 1)
            pe.wait_ge(g_ready, NG)

            def last_block(b, q, n):
                for k in range(UNITS):
                    if k < SPLIT_UNITS:
                        unit_b(b - WHOLE, k, by_turns[q])
                    else:
                        whole_unit_b(b, k, NG - 1, by_turns[q])
                    if k == SPLIT_UNITS - 2 and n is not None:
                        transpose_totals(n)

            last_block(BLOCKS - NG, 0, None)
            last_block(BLOCKS - NG + 1, 1, 0)
            with pe.Fori(0, NG // 2 - 1) as pair:
                for q in range(2):
                    last_block(pair * 2 + (q + 2 + BLOCKS - NG), q, pair * 2 + (q + 1))
            transpose_totals(NG - 1)



def kernel(x, adj, L0_gnn_h, L1_gnn_W, L1_gnn_b):
    import numpy as np
    import concourse.bacc as bacc
    from concourse.bass_utils import run_bass_kernel_spmd

    x, adj, h, w, b = (np.asarray(a) for a in (x, adj, L0_gnn_h, L1_gnn_W, L1_gnn_b))
    rows = x.shape[0]
    groups = rows // GROUP

    def by_partition(a):
        return np.ascontiguousarray(a.reshape(rows // P, P, P).transpose(1, 0, 2))

    blocks = adj.reshape(groups, GROUP, groups, UNITS, PER_UNIT, P).transpose(0, 2, 3, 5, 4, 1)
    laid = np.empty(blocks.shape, adj.dtype)
    for i in range(groups):
        for p in range(groups):
            laid[i, p] = blocks[i, (i + FIRST + p * STRIDE) % groups]
    arrays = {
        "adj_blocks": laid.reshape(groups * groups, UNITS, P, PER_UNIT * GROUP),
        "x": by_partition(x),
        "h": by_partition(h),
        "w_t": np.ascontiguousarray(w.T),
        "bias": np.ascontiguousarray(b.reshape(1, P)),
    }
    nc = bacc.Bacc("TRN2", target_bir_lowering=False, num_devices=1,
                   dynamic_dma_scratch_size=DMA_SCRATCH)
    args = [nc.dram_tensor(n, a.shape, mybir.dt.from_np(a.dtype), kind="ExternalInput").ap()
            for n, a in arrays.items()]
    shape = (P, rows // P, P)
    out = nc.dram_tensor("out", shape, mybir.dt.float32, kind="ExternalOutput").ap()
    res = nc.dram_tensor("res", shape, mybir.dt.float32, kind="Internal").ap()
    graph_kernel(nc, *args, out, res)
    got = run_bass_kernel_spmd(nc, [arrays], core_ids=[0]).results[0]["out"]
    return np.ascontiguousarray(got.transpose(1, 0, 2)).reshape(rows, P)
```
